# Optimizing a Trainium2 kernel written in Bass

```python
import numpy as np
import jax
import jax.numpy as jnp

def _softmax(x, axis=-1):
    return jax.nn.softmax(x, axis=axis)

def _gelu(x):
    return jax.nn.gelu(x, approximate=True)

def _silu(x):
    return jax.nn.silu(x)

def _sigmoid(x):
    return jax.nn.sigmoid(x)

def _layernorm(x, axis=-1, eps=1e-05):
    m = jnp.mean(x, axis=axis, keepdims=True)
    v = jnp.var(x, axis=axis, keepdims=True)
    return (x - m) / jnp.sqrt(v + eps)

def _scatter_add(tgt, idx, src, axis=0):
    return tgt.at[idx].add(src)

def _segment_sum(src, seg, n):
    return jax.ops.segment_sum(src, seg, n)
kernel_name = 'mk_dlrm_tower_d1_rec_r8_18a944'

def setup_inputs(seed: int=0):
    np.random.seed(seed)
    _w = jnp.asarray

    def _rec_inputs():
        import jax
        import jax.numpy as jnp
        _tk = jax.random.key(seed)
        dense_ctx = jax.random.normal(jax.random.fold_in(_tk, 190), (512, 16), jnp.float32)
        ids = jnp.stack([jax.random.randint(jax.random.fold_in(_tk, 200 + f), (512,), 0, v, jnp.int32) for f, v in enumerate([1250, 12500, 1250, 1250, 1000, 1250, 12500, 1000, 1000, 12500, 12500, 125000, 125000, 125000, 12500, 1250, 1000, 1250, 1250, 1250, 12500, 12500, 1250, 1250, 1250, 1000, 1250, 1250, 1250, 1000, 1250, 1000])], axis=1)
        tbl_0 = 0.05 * jax.random.normal(jax.random.fold_in(_tk, 500 + 0), (1250, 64), jnp.float32)
        tbl_1 = 0.05 * jax.random.normal(jax.random.fold_in(_tk, 500 + 1), (12500, 64), jnp.float32)
        tbl_2 = 0.05 * jax.random.normal(jax.random.fold_in(_tk, 500 + 2), (1250, 64), jnp.float32)
        tbl_3 = 0.05 * jax.random.normal(jax.random.fold_in(_tk, 500 + 3), (1250, 64), jnp.float32)
        tbl_4 = 0.05 * jax.random.normal(jax.random.fold_in(_tk, 500 + 4), (1000, 64), jnp.float32)
        tbl_5 = 0.05 * jax.random.normal(jax.random.fold_in(_tk, 500 + 5), (1250, 64), jnp.float32)
        tbl_6 = 0.05 * jax.random.normal(jax.random.fold_in(_tk, 500 + 6), (12500, 64), jnp.float32)
        tbl_7 = 0.05 * jax.random.normal(jax.random.fold_in(_tk, 500 + 7), (1000, 64), jnp.float32)
        tbl_8 = 0.05 * jax.random.normal(jax.random.fold_in(_tk, 500 + 8), (1000, 64), jnp.float32)
        tbl_9 = 0.05 * jax.random.normal(jax.random.fold_in(_tk, 500 + 9), (12500, 64), jnp.float32)
        tbl_10 = 0.05 * jax.random.normal(jax.random.fold_in(_tk, 500 + 10), (12500, 64), jnp.float32)
        tbl_11 = 0.05 * jax.random.normal(jax.random.fold_in(_tk, 500 + 11), (125000, 64), jnp.float32)
        tbl_12 = 0.05 * jax.random.normal(jax.random.fold_in(_tk, 500 + 12), (125000, 64), jnp.float32)
        tbl_13 = 0.05 * jax.random.normal(jax.random.fold_in(_tk, 500 + 13), (125000, 64), jnp.float32)
        tbl_14 = 0.05 * jax.random.normal(jax.random.fold_in(_tk, 500 + 14), (12500, 64), jnp.float32)
        tbl_15 = 0.05 * jax.random.normal(jax.random.fold_in(_tk, 500 + 15), (1250, 64), jnp.float32)
        tbl_16 = 0.05 * jax.random.normal(jax.random.fold_in(_tk, 500 + 16), (1000, 64), jnp.float32)
        tbl_17 = 0.05 * jax.random.normal(jax.random.fold_in(_tk, 500 + 17), (1250, 64), jnp.float32)
        tbl_18 = 0.05 * jax.random.normal(jax.random.fold_in(_tk, 500 + 18), (1250, 64), jnp.float32)
        tbl_19 = 0.05 * jax.random.normal(jax.random.fold_in(_tk, 500 + 19), (1250, 64), jnp.float32)
        tbl_20 = 0.05 * jax.random.normal(jax.random.fold_in(_tk, 500 + 20), (12500, 64), jnp.float32)
        tbl_21 = 0.05 * jax.random.normal(jax.random.fold_in(_tk, 500 + 21), (12500, 64), jnp.float32)
        tbl_22 = 0.05 * jax.random.normal(jax.random.fold_in(_tk, 500 + 22), (1250, 64), jnp.float32)
        tbl_23 = 0.05 * jax.random.normal(jax.random.fold_in(_tk, 500 + 23), (1250, 64), jnp.float32)
        tbl_24 = 0.05 * jax.random.normal(jax.random.fold_in(_tk, 500 + 24), (1250, 64), jnp.float32)
        tbl_25 = 0.05 * jax.random.normal(jax.random.fold_in(_tk, 500 + 25), (1000, 64), jnp.float32)
        tbl_26 = 0.05 * jax.random.normal(jax.random.fold_in(_tk, 500 + 26), (1250, 64), jnp.float32)
        tbl_27 = 0.05 * jax.random.normal(jax.random.fold_in(_tk, 500 + 27), (1250, 64), jnp.float32)
        tbl_28 = 0.05 * jax.random.normal(jax.random.fold_in(_tk, 500 + 28), (1250, 64), jnp.float32)
        tbl_29 = 0.05 * jax.random.normal(jax.random.fold_in(_tk, 500 + 29), (1000, 64), jnp.float32)
        tbl_30 = 0.05 * jax.random.normal(jax.random.fold_in(_tk, 500 + 30), (1250, 64), jnp.float32)
        tbl_31 = 0.05 * jax.random.normal(jax.random.fold_in(_tk, 500 + 31), (1000, 64), jnp.float32)
        _rk = jax.random.fold_in(_tk, 7)
        W_top1 = 0.0441942 * jax.random.normal(jax.random.fold_in(_tk, 801), (512, 512), jnp.float32)
        W_top2 = 0.0441942 * jax.random.normal(jax.random.fold_in(_tk, 802), (512, 256), jnp.float32)
        W_top3 = 0.0625 * jax.random.normal(jax.random.fold_in(_tk, 803), (256, 1), jnp.float32)
        b_top1 = jnp.zeros((512,), jnp.float32)
        b_top2 = jnp.zeros((256,), jnp.float32)
        return (dense_ctx, ids, tbl_0, tbl_1, tbl_2, tbl_3, tbl_4, tbl_5, tbl_6, tbl_7, tbl_8, tbl_9, tbl_10, tbl_11, tbl_12, tbl_13, tbl_14, tbl_15, tbl_16, tbl_17, tbl_18, tbl_19, tbl_20, tbl_21, tbl_22, tbl_23, tbl_24, tbl_25, tbl_26, tbl_27, tbl_28, tbl_29, tbl_30, tbl_31, W_top1, b_top1, W_top2, b_top2, W_top3)
    dense_ctx, ids, tbl_0, tbl_1, tbl_2, tbl_3, tbl_4, tbl_5, tbl_6, tbl_7, tbl_8, tbl_9, tbl_10, tbl_11, tbl_12, tbl_13, tbl_14, tbl_15, tbl_16, tbl_17, tbl_18, tbl_19, tbl_20, tbl_21, tbl_22, tbl_23, tbl_24, tbl_25, tbl_26, tbl_27, tbl_28, tbl_29, tbl_30, tbl_31, W_top1, b_top1, W_top2, b_top2, W_top3 = _rec_inputs()

    def _L0_rec_setup():
        import jax, jax.numpy as jnp
        import numpy as np
        BATCH = 1024
        NUM_FIELDS = 32
        EMBED_DIM = 64
        NUM_IX = NUM_FIELDS * (NUM_FIELDS - 1) // 2
        key = jax.random.key(seed)
        kx, kk = jax.random.split(key)
        x = jax.random.normal(kx, (BATCH, NUM_FIELDS, EMBED_DIM), dtype=jnp.float32)
        fan = EMBED_DIM + EMBED_DIM
        limit = float(np.sqrt(6.0 / fan))
        kernel = jax.random.uniform(kk, (EMBED_DIM, NUM_IX, EMBED_DIM), dtype=jnp.float32, minval=-limit, maxval=limit)
        return {'x': x, 'kernel': kernel}
    _L0_rec_all = _L0_rec_setup()
    _L0_rec_in = {k: v for k, v in _L0_rec_all.items() if k in ('kernel',)}
    del _L0_rec_all
    return {'dense_ctx': dense_ctx, 'ids': ids, 'tbl_0': tbl_0, 'tbl_1': tbl_1, 'tbl_2': tbl_2, 'tbl_3': tbl_3, 'tbl_4': tbl_4, 'tbl_5': tbl_5, 'tbl_6': tbl_6, 'tbl_7': tbl_7, 'tbl_8': tbl_8, 'tbl_9': tbl_9, 'tbl_10': tbl_10, 'tbl_11': tbl_11, 'tbl_12': tbl_12, 'tbl_13': tbl_13, 'tbl_14': tbl_14, 'tbl_15': tbl_15, 'tbl_16': tbl_16, 'tbl_17': tbl_17, 'tbl_18': tbl_18, 'tbl_19': tbl_19, 'tbl_20': tbl_20, 'tbl_21': tbl_21, 'tbl_22': tbl_22, 'tbl_23': tbl_23, 'tbl_24': tbl_24, 'tbl_25': tbl_25, 'tbl_26': tbl_26, 'tbl_27': tbl_27, 'tbl_28': tbl_28, 'tbl_29': tbl_29, 'tbl_30': tbl_30, 'tbl_31': tbl_31, 'W_top1': W_top1, 'b_top1': b_top1, 'W_top2': W_top2, 'b_top2': b_top2, 'W_top3': W_top3, 'L0_rec_kernel': _L0_rec_in['kernel']}

def reference(dense_ctx, ids, tbl_0, tbl_1, tbl_2, tbl_3, tbl_4, tbl_5, tbl_6, tbl_7, tbl_8, tbl_9, tbl_10, tbl_11, tbl_12, tbl_13, tbl_14, tbl_15, tbl_16, tbl_17, tbl_18, tbl_19, tbl_20, tbl_21, tbl_22, tbl_23, tbl_24, tbl_25, tbl_26, tbl_27, tbl_28, tbl_29, tbl_30, tbl_31, W_top1, b_top1, W_top2, b_top2, W_top3, L0_rec_kernel):
    import jax
    import jax.numpy as jnp

    def _L0_rec_ref(x, kernel):
        import jax, jax.numpy as jnp
        import numpy as np
        BATCH = 1024
        NUM_FIELDS = 32
        EMBED_DIM = 64
        NUM_IX = NUM_FIELDS * (NUM_FIELDS - 1) // 2
        num_fields = x.shape[1]
        row, col = np.triu_indices(num_fields, k=1)
        p = x[:, row]
        q = x[:, col]
        out = jnp.einsum('bni,oni,bno->bn', p, kernel, q)
        return out
    e = jnp.stack([tbl_0[ids[:, 0]], tbl_1[ids[:, 1]], tbl_2[ids[:, 2]], tbl_3[ids[:, 3]], tbl_4[ids[:, 4]], tbl_5[ids[:, 5]], tbl_6[ids[:, 6]], tbl_7[ids[:, 7]], tbl_8[ids[:, 8]], tbl_9[ids[:, 9]], tbl_10[ids[:, 10]], tbl_11[ids[:, 11]], tbl_12[ids[:, 12]], tbl_13[ids[:, 13]], tbl_14[ids[:, 14]], tbl_15[ids[:, 15]], tbl_16[ids[:, 16]], tbl_17[ids[:, 17]], tbl_18[ids[:, 18]], tbl_19[ids[:, 19]], tbl_20[ids[:, 20]], tbl_21[ids[:, 21]], tbl_22[ids[:, 22]], tbl_23[ids[:, 23]], tbl_24[ids[:, 24]], tbl_25[ids[:, 25]], tbl_26[ids[:, 26]], tbl_27[ids[:, 27]], tbl_28[ids[:, 28]], tbl_29[ids[:, 29]], tbl_30[ids[:, 30]], tbl_31[ids[:, 31]]], axis=1)
    z = _L0_rec_ref(e, L0_rec_kernel)
    z = z.reshape(z.shape[0], -1)
    h = jnp.concatenate([z, dense_ctx], axis=1)
    h = jnp.maximum(h @ W_top1 + b_top1, 0.0)
    h = jnp.maximum(h @ W_top2 + b_top2, 0.0)
    y = h @ W_top3
    return y

_drawn_inputs = setup_inputs


def setup_inputs(seed=0):
    import zlib

    import numpy as np

    out = dict(_drawn_inputs(seed))
    spreads = {'b_top1': (0.0, 0.1), 'b_top2': (0.0, 0.1)}
    factors = {}
    for name, (base, spread) in spreads.items():
        noise = np.random.default_rng([zlib.crc32(name.encode()), seed]).standard_normal(out[name].shape)
        drawn = base * np.exp(spread * noise) if base else spread * noise
        out[name] = jnp.asarray(drawn.astype(out[name].dtype))
    for name, factor in factors.items():
        out[name] = (out[name] * factor).astype(out[name].dtype)
    return out
```

```python
from contextlib import ExitStack

import numpy as np

import concourse.bass as bass
from concourse import mybir
from concourse.alu_op_type import AluOpType as ALU

F32, F32R, I32 = mybir.dt.float32, mybir.dt.float32r, mybir.dt.int32
ACT = mybir.ActivationFunctionType

P = 128
BATCH, FIELDS, EMBED = 512, 32, 64
DENSE, HID1, HID2 = 16, 512, 256
NB = BATCH // P
GROUPS = FIELDS // 2
PSUM_BANKS, BANK = 8, 512

BLOCKS = [(j, pair) for j in range(1, FIELDS) for pair in range((j + 1) // 2)]
NBLOCKS = len(BLOCKS)
UNIT = 2
UNITS = [(j, pair, min(UNIT, (j + 1) // 2 - pair)) for j in range(1, FIELDS)
         for pair in range(0, (j + 1) // 2, UNIT)]
NUNITS = len(UNITS)
FIRST_BLOCK = [sum(u[2] for u in UNITS[:k]) for k in range(NUNITS + 1)]
UNITS_THROUGH = [sum(u[0] <= j for u in UNITS) for j in range(FIELDS)]

CHUNK = 64
CHUNKS = NBLOCKS // CHUNK
STRIPS = 4
SEL_W = 62

K_GROUP = 16
K_GROUPS = NBLOCKS // K_GROUP
K_STAGES = 3
K_RING = 8
M_RING = 3
T_RING = 3
P_RING = 6
LAG = 2
EARLY = 10


def unit_of_block(t):
    return next(k for k in range(NUNITS) if FIRST_BLOCK[k + 1] > t)


OPERANDS_AFTER = {-1: [0, 1]}
for _f in range(2, FIELDS):
    _last = UNITS_THROUGH[_f - 1] - 1
    _first = UNITS_THROUGH[_f - 2]
    OPERANDS_AFTER.setdefault(_last if _f <= EARLY else (_first + _last) // 2, []).append(_f)
SPLIT_AFTER = {-1: [0, 1]}
for _g in range(2, K_GROUPS):
    _at = UNITS_THROUGH[_g - 1] - 1 if _g < K_RING else unit_of_block(K_GROUP * (_g - K_RING + 1) + 8)
    SPLIT_AFTER.setdefault(_at, []).append(_g)


def tower(nc, ids, tables, kernel_t, consts, w1, dense_t, b1, w2, b2, w3, y):
    ctx = ExitStack()
    with ctx:
        def sb(name, shape, dt=F32):
            return ctx.enter_context(nc.sbuf_tensor(name, shape, dt))

        def ps(name, shape):
            return ctx.enter_context(nc.psum_tensor(name, shape, F32))

        def sem(name):
            return ctx.enter_context(nc.semaphore(name))

        idx = sb("idx", [P, FIELDS * NB], I32)
        rows = sb("rows", [P, FIELDS, NB, EMBED])
        const = sb("const", [P, P + SEL_W])
        identity, selector = const[:, 0:P], const[:, P:P + SEL_W]
        rows_twice = sb("rows_twice", [P, 2, NB, 2, EMBED])
        e_pair = sb("e_pair", [P, GROUPS, BATCH])
        e_hi = sb("e_hi", [P, M_RING, BATCH], F32R)
        e_lo = sb("e_lo", [P, M_RING, BATCH], F32R)
        k_stage = sb("k_stage", [P, K_STAGES, K_GROUP // 2, P])
        k_split = sb("k_split", [P, K_RING * K_GROUP // 2, 2, P], F32R)
        prod = sb("prod", [P, P_RING, UNIT * BATCH])
        z_sb = sb("z_sb", [P, CHUNKS, BATCH])
        dense_sb = sb("dense_sb", [P, BATCH])
        w1_sb = sb("w1_sb", [P, CHUNKS + 1, HID1])
        w2_sb = sb("w2_sb", [P, HID1 // P, HID2])
        w3_sb = sb("w3_sb", [P, HID2 // P])
        b1_sb = sb("b1_sb", [P, HID1 // P])
        b2_sb = sb("b2_sb", [P, HID2 // P])
        h1_sb = rows[:, 0:8].rearrange("p (m f) t e -> p m (f t e)", m=4)
        h2_sb = rows[:, 8:12].rearrange("p (m f) t e -> p m (f t e)", m=2)
        y_sb = rows[0:1, 12:14].rearrange("p f t e -> p (f t e)")

        t_ps = ps("t_ps", [P, T_RING * UNIT, BANK])
        tr_ps = ps("tr_ps", [P, NB, P])
        z_ps = ps("z_ps", [P, BANK])

        ids_arrived = sem("ids_arrived")
        const_arrived = sem("const_arrived")
        weights_arrived = sem("weights_arrived")
        rows_arrived = [sem(f"rows_arrived_{f}") for f in range(FIELDS)]
        k_arrived = [sem(f"k_arrived_{s}") for s in range(K_STAGES)]
        k_hi_done = sem("k_hi_done")
        k_lo_done = sem("k_lo_done")
        doubled = sem("doubled")
        transposed = sem("transposed")
        e_hi_done = sem("e_hi_done")
        e_pair_done = sem("e_pair_done")
        e_lo_done = sem("e_lo_done")
        t_done = sem("t_done")
        prod_done = sem("prod_done")
        summed = sem("summed")
        z_done = sem("z_done")
        h1_ready, h1_act = sem("h1_ready"), sem("h1_act")
        h2_ready, h2_act = sem("h2_ready"), sem("h2_act")
        y_ready, y_done, y_stored = sem("y_ready"), sem("y_done"), sem("y_stored")
        block = ctx.enter_context(nc.Block())

        def halves(g):
            ring = (g % K_RING) * (K_GROUP // 2)
            at = slice(ring, ring + K_GROUP // 2)
            return g % K_STAGES, at, ((slice(0, 64), slice(64, 128), 0), (slice(64, 128), slice(0, 64), 1))

        def freed_units(g):
            return unit_of_block(K_GROUP * (g - K_RING + 1) - 1) + 1

        @block.sync
        def _(sp):
            sp.dma_start(idx[:], ids).then_inc(ids_arrived, 16)
            sp.dma_start(const[:], consts).then_inc(const_arrived, 16)
            for g in range(K_GROUPS):
                if g >= K_STAGES:
                    sp.wait_ge(k_lo_done, 2 * (g - K_STAGES + 1))
                n = K_GROUP // 2
                sp.dma_start(k_stage[:, g % K_STAGES], kernel_t[:, g * n:(g + 1) * n, :]).then_inc(
                    k_arrived[g % K_STAGES], 16)
                if g == K_STAGES:
                    for dst, src in ((w1_sb, w1), (w2_sb, w2), (w3_sb, w3), (b1_sb, b1), (b2_sb, b2),
                                     (dense_sb, dense_t)):
                        sp.dma_start(dst[:], src).then_inc(weights_arrived, 16)
            sp.wait_ge(y_done, 1)
            sp.dma_start(y, y_sb).then_inc(y_stored, 16)
            sp.wait_ge(y_stored, 16)

        @block.gpsimd
        def _(pool):
            pool.wait_ge(ids_arrived, 16)
            for f in range(FIELDS):
                for t in range(NB):
                    at = f * NB + t
                    nc.gpsimd.indirect_dma_start(
                        out=rows[:, f, t, :], out_offset=None, in_=tables[f],
                        in_offset=bass.IndirectOffsetOnAxis(ap=idx[:, at:at + 1], axis=0),
                    ).then_inc(rows_arrived[f], 16)

        @block.scalar
        def _(act):
            def operands(f):
                act.wait_ge(rows_arrived[f], 16 * NB)
                if f >= 2:
                    act.wait_ge(transposed, f - 1)
                nc.scalar.copy(rows_twice[:, f % 2],
                               rows[:, f].unsqueeze(2).broadcast_to([P, NB, 2, EMBED])).then_inc(doubled, 1)
                act.wait_ge(transposed, f + 1)
                half = slice(64 * (f % 2), 64 * (f % 2) + 64)
                nc.scalar.copy(e_pair[half, f // 2, :], tr_ps[half].rearrange("p t b -> p (t b)")).then_inc(
                    e_pair_done, 1)
                if f >= 1:
                    if f > M_RING:
                        act.wait_ge(t_done, UNITS_THROUGH[f - M_RING])
                    nc.scalar.copy(e_hi[:, f % M_RING, :], tr_ps[:].rearrange("p t b -> p (t b)")).then_inc(
                        e_hi_done, 1)

            def split(g):
                stage, at, parts = halves(g)
                act.wait_ge(k_arrived[stage], 16 * (g // K_STAGES + 1))
                if g >= K_RING:
                    act.wait_ge(t_done, freed_units(g))
                for here, _, col in parts:
                    nc.scalar.copy(k_split[here, at, col, :], k_stage[here, stage]).then_inc(k_hi_done, 1)

            for k in range(-1, NUNITS):
                for g in SPLIT_AFTER.get(k, ()):
                    split(g)
                for f in OPERANDS_AFTER.get(k, ()):
                    operands(f)
                done = FIRST_BLOCK[max(k - LAG, 0)] // CHUNK
                before = FIRST_BLOCK[max(k - 1 - LAG, 0)] // CHUNK
                for c in range(before, done):
                    act.wait_ge(summed, (c + 1) * CHUNK // STRIPS)
                    nc.scalar.copy(z_sb[:, c, :], z_ps[:]).then_inc(z_done, 1)
            act.wait_ge(summed, NBLOCKS // STRIPS)
            nc.scalar.copy(z_sb[:, CHUNKS - 1, :], z_ps[:]).then_inc(z_done, 1)

            act.wait_ge(weights_arrived, 16 * 6)
            for m in range(0, HID1 // P, 2):
                act.wait_ge(h1_ready, m + 1)
                nc.scalar.activation(h1_sb[:, m, :], t_ps[:, m, :], ACT.Relu, bias=b1_sb[:, m:m + 1]).then_inc(
                    h1_act, 1)
            act.wait_ge(h2_ready, 1)
            nc.scalar.activation(h2_sb[:, 0, :], t_ps[:, 4, :], ACT.Relu, bias=b2_sb[:, 0:1]).then_inc(h2_act, 1)
            act.wait_ge(y_ready, 1)
            nc.scalar.copy(y_sb, z_ps[0:1, :]).then_inc(y_done, 1)

        @block.vector
        def _(dve):
            def operands(f):
                if f >= 1:
                    dve.wait_ge(e_hi_done, f)
                    nc.vector.tensor_tensor(
                        e_lo[:, f % M_RING, :], tr_ps[:].rearrange("p t b -> p (t b)"),
                        e_hi[:, f % M_RING, :].bitcast(F32), ALU.subtract).then_inc(e_lo_done, 1)

            def split(g):
                stage, at, parts = halves(g)
                for n, (here, there, col) in enumerate(parts):
                    dve.wait_ge(k_hi_done, 2 * g + n + 1)
                    nc.vector.tensor_tensor(k_split[there, at, col, :], k_stage[here, stage],
                                            k_split[here, at, col, :].bitcast(F32),
                                            ALU.subtract).then_inc(k_lo_done, 1)

            for k in range(-1, NUNITS):
                if k >= 0:
                    j, pair, n = UNITS[k]
                    if pair + n == (j + 1) // 2 or pair == 0:
                        dve.wait_ge(e_pair_done, min(2 * (pair + n), j + 1))
                    if k >= P_RING:
                        dve.wait_ge(summed, -(-FIRST_BLOCK[k - P_RING + 1] // STRIPS))
                    dve.wait_ge(t_done, k + 1)
                    bank = UNIT * (k % T_RING)
                    nc.vector.tensor_tensor(
                        prod[:, k % P_RING, 0:n * BATCH], t_ps[:, bank:bank + n, :].rearrange("p n b -> p (n b)"),
                        e_pair[:, pair:pair + n, :].rearrange("p n b -> p (n b)"), ALU.mult).then_inc(prod_done, 1)
                for f in OPERANDS_AFTER.get(k, ()):
                    operands(f)
                for g in SPLIT_AFTER.get(k, ()):
                    split(g)

            dve.wait_ge(weights_arrived, 16 * 6)
            for m in range(1, HID1 // P, 2):
                dve.wait_ge(h1_ready, m + 1)
                nc.vector.tensor_scalar(h1_sb[:, m, :], t_ps[:, m, :], b1_sb[:, m:m + 1], 0.0, ALU.add,
                                        ALU.max).then_inc(h1_act, 1)
            dve.wait_ge(h2_ready, 2)
            nc.vector.tensor_scalar(h2_sb[:, 1, :], t_ps[:, 5, :], b2_sb[:, 1:2], 0.0, ALU.add,
                                    ALU.max).then_inc(h2_act, 1)

        @block.tensor
        def _(pe):
            def transpose(f):
                if f >= 1:
                    pe.wait_ge(e_pair_done, f)
                if f >= 2:
                    pe.wait_ge(e_lo_done, f - 1)
                pe.wait_ge(doubled, f + 1)
                for t in range(NB):
                    last = nc.tensor.transpose(tr_ps[:, t, :], rows_twice[:, f % 2, t].rearrange("p h e -> p (h e)"),
                                               identity)
                last.then_inc(transposed, 1)

            def sum_up(first):
                chunk, within = divmod(first, CHUNK)
                if chunk and not within:
                    pe.wait_ge(z_done, chunk)
                pe.wait_ge(prod_done, unit_of_block(first + STRIPS - 1) + 1)
                r = within // STRIPS
                for s in range(STRIPS):
                    k = unit_of_block(first + s)
                    col = (first + s - FIRST_BLOCK[k]) * BATCH
                    last = nc.tensor.matmul(
                        z_ps[32 * s:32 * s + 32, :], selector[:, SEL_W - 32 - 2 * r:SEL_W - 2 * r],
                        prod[:, k % P_RING, col:col + BATCH], start=(within == 0),
                        stop=(within == CHUNK - STRIPS))
                last.then_inc(summed, 1)

            pe.wait_ge(const_arrived, 16)
            sums = 0
            for k in range(-1, NUNITS):
                if k >= 0:
                    j, pair, n = UNITS[k]
                    if pair == 0:
                        pe.wait_ge(e_lo_done, j)
                    if k >= T_RING:
                        pe.wait_ge(prod_done, k - T_RING + 1)
                    for i in range(n):
                        t = FIRST_BLOCK[k] + i
                        if t % K_GROUP == 0:
                            pe.wait_ge(k_lo_done, 2 * (t // K_GROUP + 1))
                        tile = k_split[:, t // 2 % (K_RING * K_GROUP // 2), t % 2, :]
                        bank = t_ps[:, UNIT * (k % T_RING) + i, :]
                        nc.tensor.matmul(bank, tile, e_hi[:, j % M_RING, :], start=True, stop=False)
                        last = nc.tensor.matmul(bank, tile, e_lo[:, j % M_RING, :], start=False, stop=True)
                    last.then_inc(t_done, 1)
                for f in OPERANDS_AFTER.get(k, ()):
                    transpose(f)
                while sums + STRIPS <= FIRST_BLOCK[max(k - LAG + 1, 0)]:
                    sum_up(sums)
                    sums += STRIPS
            while sums < NBLOCKS:
                sum_up(sums)
                sums += STRIPS

            pe.wait_ge(weights_arrived, 16 * 6)
            pe.wait_ge(z_done, CHUNKS)
            for m in range(HID1 // P):
                cols = slice(m * P, (m + 1) * P)
                nc.tensor.matmul(t_ps[:, m, :], w1_sb[:, CHUNKS, cols], dense_sb[:], start=True, stop=False)
                for c in range(CHUNKS):
                    last = nc.tensor.matmul(t_ps[:, m, :], w1_sb[:, c, cols], z_sb[:, c, :], start=False,
                                            stop=(c == CHUNKS - 1))
                last.then_inc(h1_ready, 1)
            pe.wait_ge(h1_act, HID1 // P)
            for m in range(HID2 // P):
                for c in range(HID1 // P):
                    last = nc.tensor.matmul(t_ps[:, 4 + m, :], w2_sb[:, c, m * P:(m + 1) * P], h1_sb[:, c, :],
                                            start=(c == 0), stop=(c == HID1 // P - 1))
                last.then_inc(h2_ready, 1)
            pe.wait_ge(h2_act, HID2 // P)
            for c in range(HID2 // P):
                last = nc.tensor.matmul(z_ps[0:1, :], w3_sb[:, c:c + 1], h2_sb[:, c, :], start=(c == 0),
                                        stop=(c == HID2 // P - 1))
            last.then_inc(y_ready, 1)


def kernel(**inputs):
    import concourse.bacc as bacc
    from concourse.bass_utils import run_bass_kernel_spmd

    pair_index = {}
    for i in range(FIELDS):
        for j in range(i + 1, FIELDS):
            pair_index[i, j] = len(pair_index)

    ids = np.asarray(inputs["ids"]).reshape(NB, P, FIELDS).transpose(1, 2, 0).reshape(P, FIELDS * NB)
    k_in = np.asarray(inputs["L0_rec_kernel"])
    w1_in = np.asarray(inputs["W_top1"])
    k_t = np.zeros((P, NBLOCKS // 2, 2, EMBED), k_in.dtype)
    w1 = np.zeros((CHUNKS + 1, P, HID1), w1_in.dtype)
    for t, (j, pair) in enumerate(BLOCKS):
        for h in range(2):
            i = 2 * pair + h
            if i < j:
                n = pair_index[i, j]
                k_t[64 * (t % 2):64 * (t % 2) + 64, t // 2, h, :] = k_in[:, n, :]
                within = t % CHUNK
                w1[t // CHUNK, 32 * (within % STRIPS) + 2 * (within // STRIPS) + h] = w1_in[n]
    w1[CHUNKS, 0:DENSE] = w1_in[len(pair_index):]
    dense_in = np.asarray(inputs["dense_ctx"])
    dense_t = np.zeros((P, BATCH), dense_in.dtype)
    dense_t[0:DENSE] = dense_in.T
    consts = np.zeros((P, P + SEL_W), np.float32)
    consts[:, 0:P] = np.eye(P)
    consts[0:64, P + 30] = 1.0
    consts[64:128, P + 31] = 1.0

    arrays = {
        "ids": ids,
        **{f"table_{f}": np.asarray(inputs[f"tbl_{f}"]) for f in range(FIELDS)},
        "kernel_t": k_t.reshape(P, NBLOCKS // 2, 2 * EMBED),
        "consts": consts,
        "w1": w1.transpose(1, 0, 2),
        "dense_t": dense_t,
        "b1": np.asarray(inputs["b_top1"]).reshape(HID1 // P, P).T,
        "w2": np.asarray(inputs["W_top2"]).reshape(HID1 // P, P, HID2).transpose(1, 0, 2),
        "b2": np.asarray(inputs["b_top2"]).reshape(HID2 // P, P).T,
        "w3": np.asarray(inputs["W_top3"]).reshape(HID2 // P, P).T,
    }
    arrays = {n: np.ascontiguousarray(a) for n, a in arrays.items()}

    nc = bacc.Bacc("TRN2", target_bir_lowering=False, num_devices=1)
    ap = {n: nc.dram_tensor(n, a.shape, mybir.dt.from_np(a.dtype), kind="ExternalInput").ap()
          for n, a in arrays.items()}
    y = nc.dram_tensor("y", (1, BATCH), F32, kind="ExternalOutput").ap()
    tower(nc, ap["ids"], [ap[f"table_{f}"] for f in range(FIELDS)], ap["kernel_t"], ap["consts"], ap["w1"],
          ap["dense_t"], ap["b1"], ap["w2"], ap["b2"], ap["w3"], y)
    result = run_bass_kernel_spmd(nc, [arrays], core_ids=[0])
    return np.asarray(result.results[0]["y"]).reshape(BATCH, 1)
```

```python
from contextlib import ExitStack

import numpy as np

import concourse.bass as bass
from concourse import mybir
from concourse.alu_op_type import AluOpType as ALU

F32, F32R, I32 = mybir.dt.float32, mybir.dt.float32r, mybir.dt.int32
ACT = mybir.ActivationFunctionType

P = 128
BATCH, FIELDS, EMBED = 512, 32, 64
DENSE, HID1, HID2 = 16, 512, 256
NB = BATCH // P
GROUPS = FIELDS // 2
PSUM_BANKS, BANK = 8, 512

BLOCKS = [(j, pair) for j in range(1, FIELDS) for pair in range((j + 1) // 2)]
NBLOCKS = len(BLOCKS)
LAYER2_ORDER = [(0, 0), (0, 1), (0, 2), (1, 0), (0, 3), (1, 1), (1, 2), (1, 3)]
UNIT = 2
UNITS = [(j, pair, min(UNIT, (j + 1) // 2 - pair)) for j in range(1, FIELDS)
         for pair in range(0, (j + 1) // 2, UNIT)]
NUNITS = len(UNITS)
FIRST_BLOCK = [sum(u[2] for u in UNITS[:k]) for k in range(NUNITS + 1)]
UNITS_THROUGH = [sum(u[0] <= j for u in UNITS) for j in range(FIELDS)]

CHUNK = 64
CHUNKS = NBLOCKS // CHUNK
STRIPS = 4
SEL_W = 62

K_GROUP = 16
K_GROUPS = NBLOCKS // K_GROUP
K_STAGES = 3
K_RING = 7
ROW_RING = 16
M_RING = 4
SPLIT_FIRST = 2
SPLIT_RING = 2
T_RING = 3
COPY_RING = 2
P_RING = 7
LAG = 4
LO_LAG = 0
LEAD = 3
EARLY = 5


WEIGHTS_AT = 10
DENSE_AT = 130


def unit_of_block(t):
    return next(k for k in range(NUNITS) if FIRST_BLOCK[k + 1] > t)


OPERANDS_AFTER, LO_AFTER = {-1: [0, 1]}, {-1: [0, 1]}
_lo_at = -1
for _f in range(2, FIELDS):
    _last = UNITS_THROUGH[_f - 1] - 1
    _at = _last if _f <= EARLY else max(_last - LEAD, _lo_at)
    OPERANDS_AFTER.setdefault(_at, []).append(_f)
    _lo_at = min(_at + LO_LAG, _last)
    LO_AFTER.setdefault(_lo_at, []).append(_f)
SPLIT_AFTER = {}
for _g in range(SPLIT_FIRST, K_GROUPS):
    _at = UNITS_THROUGH[_g - 1] - 1 if _g < K_RING else unit_of_block(K_GROUP * (_g - K_RING + 1) + 8)
    SPLIT_AFTER.setdefault(_at, []).append(_g)


def summed_after(k):
    now, before = (FIRST_BLOCK[max(i - LAG + 1, 0)] // STRIPS * STRIPS for i in (k, k - 1))
    if now // CHUNK > before // CHUNK:
        now = now // CHUNK * CHUNK
    return now


FIRST_ON_POOL = 75
POOL_EVERY = 4


def on_pool(k):
    return k >= FIRST_ON_POOL and k % POOL_EVERY == POOL_EVERY - 1


def pool_units(k):
    return sum(on_pool(i) for i in range(k + 1))


def dve_units(k):
    return k + 1 - pool_units(k)


def tower(nc, ids, tables, kernel_t, consts, w1, dense_t, b1, w2, b2, w3, y):
    ctx = ExitStack()
    with ctx:
        def sb(name, shape, dt=F32):
            return ctx.enter_context(nc.sbuf_tensor(name, shape, dt))

        def ps(name, shape):
            return ctx.enter_context(nc.psum_tensor(name, shape, F32))

        def sem(name):
            return ctx.enter_context(nc.semaphore(name))

        idx = sb("idx", [P, FIELDS * NB], I32)
        rows = sb("rows", [P, ROW_RING, NB, EMBED])
        const = sb("const", [P, P + SEL_W])
        identity, selector = const[:, 0:P], const[:, P:P + SEL_W]
        rows_twice = sb("rows_twice", [P, 2, NB, 2, EMBED])
        e_pair = sb("e_pair", [P, GROUPS, BATCH])
        e_hi = sb("e_hi", [P, M_RING, BATCH], F32R)
        e_lo = sb("e_lo", [P, M_RING, BATCH], F32R)
        k_stage = sb("k_stage", [P, K_STAGES, K_GROUP // 2, P])
        k_hi = sb("k_hi", [P, SPLIT_RING, K_GROUP // 2, P], F32R)
        k_split = sb("k_split", [P, 2, K_RING * K_GROUP // 2, P], F32R)
        t_copy = sb("t_copy", [P, COPY_RING, UNIT * BATCH])
        prod = sb("prod", [P, P_RING, UNIT * BATCH])
        z_sb = sb("z_sb", [P, CHUNKS, BATCH])
        dense_sb = sb("dense_sb", [P, BATCH])
        w1_sb = sb("w1_sb", [P, CHUNKS + 1, HID1])
        w2_sb = sb("w2_sb", [P, HID1 // P, HID2])
        w3_sb = sb("w3_sb", [P, HID2 // P])
        b1_sb = sb("b1_sb", [P, HID1 // P])
        b2_sb = sb("b2_sb", [P, HID2 // P])
        h1_sb = rows[:, 0:8].rearrange("p (m f) t e -> p m (f t e)", m=4)
        h2_sb = rows[:, 8:12].rearrange("p (m f) t e -> p m (f t e)", m=2)
        free_split = k_hi[:, (K_GROUPS - 2) % SPLIT_RING].rearrange("p t c -> p (t c)")
        dense_split, w1_split = free_split[:, 0:BATCH], free_split[:, BATCH:BATCH + HID1]
        y_sb = dense_sb[0:1, :]

        t_ps = ps("t_ps", [P, T_RING * UNIT, BANK])
        tr_ps = ps("tr_ps", [P, NB, P])
        z_ps = ps("z_ps", [P, BANK])
        h1_ps = [tr_ps[:].rearrange("p t b -> p (t b)")] + [t_ps[:, m, :] for m in range(1, HID1 // P)]
        h2_ps = [t_ps[:, 4, :], t_ps[:, 5, :]]

        ids_arrived = sem("ids_arrived")
        const_arrived = sem("const_arrived")
        weights_arrived = sem("weights_arrived")
        rows_arrived = [sem(f"rows_arrived_{f}") for f in range(FIELDS)]
        k_arrived = [sem(f"k_arrived_{s}") for s in range(K_STAGES)]
        k_hi_done = sem("k_hi_done")
        k_lo_done = sem("k_lo_done")
        k_spread = [sem(f"k_spread_{s}") for s in range(K_STAGES)]
        doubled = sem("doubled")
        transposed = sem("transposed")
        e_hi_done = sem("e_hi_done")
        e_pair_done = sem("e_pair_done")
        e_lo_done = sem("e_lo_done")
        t_done = sem("t_done")
        t_copied = sem("t_copied")
        prod_done = sem("prod_done")
        pool_prod_done = sem("pool_prod_done")
        summed = sem("summed")
        z_done = sem("z_done")
        dense_hi_done, dense_lo_done = sem("dense_hi_done"), sem("dense_lo_done")
        h1_ready, h1_act = sem("h1_ready"), [sem(f"h1_act_{m}") for m in range(HID1 // P)]
        h2_ready, h2_act = sem("h2_ready"), [sem(f"h2_act_{m}") for m in range(HID2 // P)]
        y_ready, y_done, y_stored = sem("y_ready"), sem("y_done"), sem("y_stored")
        block = ctx.enter_context(nc.Block())

        upper, lower = slice(0, 64), slice(64, 128)

        def ring_of(g):
            first = (g % K_RING) * (K_GROUP // 2)
            return slice(first, first + K_GROUP // 2)

        def wait_for_k(engine, g):
            engine.wait_ge(k_spread[g % K_STAGES], 16 * 4 * (g // K_STAGES + 1))

        def wait_for_sum(engine, k):
            if k >= P_RING:
                engine.wait_ge(summed, -(-FIRST_BLOCK[k - P_RING + 1] // STRIPS))

        def freed_units(g):
            return unit_of_block(K_GROUP * (g - K_RING + 1) - 1) + 1

        @block.sync
        def _(sp):
            sp.dma_start(idx[:], ids).then_inc(ids_arrived, 16)
            sp.dma_start(const[:], consts).then_inc(const_arrived, 16)
            def load(g):
                n = K_GROUP // 2
                if g >= K_STAGES:
                    wait_for_k(sp, g - K_STAGES)
                sp.dma_start(k_stage[:, g % K_STAGES], kernel_t[:, g * n:(g + 1) * n, :]).then_inc(
                    k_arrived[g % K_STAGES], 16)

            def spread_kernel(g):
                at, stage, done = ring_of(g), g % K_STAGES, k_spread[g % K_STAGES]
                k_raw, hi = k_split[:].bitcast(F32), k_hi[:].bitcast(F32)
                if g >= K_RING:
                    sp.wait_ge(t_done, freed_units(g))
                sp.wait_ge(k_hi_done, g + 1)
                sp.dma_start(k_raw[upper, 0, at, :], hi[upper, g % SPLIT_RING]).then_inc(done, 16)
                sp.dma_start(k_raw[lower, 1, at, :], hi[lower, g % SPLIT_RING]).then_inc(done, 16)
                sp.wait_ge(k_lo_done, g + 1)
                sp.dma_start(k_raw[lower, 0, at, :], k_stage[upper, stage]).then_inc(done, 16)
                sp.dma_start(k_raw[upper, 1, at, :], k_stage[lower, stage]).then_inc(done, 16)

            for g in range(K_STAGES):
                load(g)
            for g in range(K_GROUPS):
                spread_kernel(g)
                if 0 <= g - 1 < K_GROUPS - K_STAGES:
                    load(g - 1 + K_STAGES)
                if g == WEIGHTS_AT:
                    for dst, src in ((w1_sb, w1), (w2_sb, w2), (w3_sb, w3), (b1_sb, b1), (b2_sb, b2),
                                     (dense_sb, dense_t)):
                        sp.dma_start(dst[:], src).then_inc(weights_arrived, 16)
            sp.wait_ge(y_done, 1)
            sp.dma_start(y, y_sb).then_inc(y_stored, 16)
            sp.wait_ge(y_stored, 16)

        @block.gpsimd
        def _(pool):
            pool.wait_ge(ids_arrived, 16)
            for f in range(FIELDS):
                if f >= ROW_RING:
                    pool.wait_ge(doubled, f - ROW_RING + 1)
                for t in range(NB):
                    at = f * NB + t
                    nc.gpsimd.indirect_dma_start(
                        out=rows[:, f % ROW_RING, t, :], out_offset=None, in_=tables[f],
                        in_offset=bass.IndirectOffsetOnAxis(ap=idx[:, at:at + 1], axis=0),
                    ).then_inc(rows_arrived[f], 16)
            for f in range(FIELDS):
                pool.wait_ge(rows_arrived[f], 16 * NB)
            for k in range(NUNITS):
                if on_pool(k):
                    j, pair, n = UNITS[k]
                    pool.wait_ge(t_copied, pool_units(k))
                    wait_for_sum(pool, k)
                    nc.gpsimd.tensor_tensor(
                        prod[:, k % P_RING, 0:n * BATCH], t_copy[:, pool_units(k) % COPY_RING, 0:n * BATCH],
                        e_pair[:, pair:pair + n, :].rearrange("p n b -> p (n b)"), ALU.mult).then_inc(
                            pool_prod_done, 1)

        @block.scalar
        def _(act):
            def double(f):
                act.wait_ge(rows_arrived[f], 16 * NB)
                if f >= 2:
                    act.wait_ge(transposed, f - 1)
                nc.scalar.copy(rows_twice[:, f % 2],
                               rows[:, f % ROW_RING].unsqueeze(2).broadcast_to([P, NB, 2, EMBED])).then_inc(doubled, 1)

            def operands(f):
                act.wait_ge(transposed, f + 1)
                half = slice(64 * (f % 2), 64 * (f % 2) + 64)
                nc.scalar.copy(e_pair[half, f // 2, :], tr_ps[half].rearrange("p t b -> p (t b)")).then_inc(
                    e_pair_done, 1)
                if f >= 1:
                    if f > M_RING:
                        act.wait_ge(t_done, UNITS_THROUGH[f - M_RING])
                    nc.scalar.copy(e_hi[:, f % M_RING, :], tr_ps[:].rearrange("p t b -> p (t b)")).then_inc(
                        e_hi_done, 1)

            def split(g):
                stage = g % K_STAGES
                act.wait_ge(k_arrived[stage], 16 * (g // K_STAGES + 1))
                if g >= SPLIT_RING:
                    wait_for_k(act, g - SPLIT_RING)
                nc.scalar.copy(k_hi[:, g % SPLIT_RING], k_stage[:, stage]).then_inc(k_hi_done, 1)

            for g in range(SPLIT_FIRST):
                split(g)
            def evacuate(c):
                act.wait_ge(summed, (c + 1) * CHUNK // STRIPS)
                nc.scalar.copy(z_sb[:, c, :], z_ps[:]).then_inc(z_done, 1)

            double(0)
            for k in range(-1, NUNITS):
                if k >= 0 and on_pool(k):
                    n = UNITS[k][2]
                    bank = UNIT * (k % T_RING)
                    act.wait_ge(t_done, k + 1)
                    if pool_units(k) > COPY_RING:
                        act.wait_ge(pool_prod_done, pool_units(k) - COPY_RING)
                    nc.scalar.copy(t_copy[:, pool_units(k) % COPY_RING, 0:n * BATCH],
                                   t_ps[:, bank:bank + n, :].rearrange("p n b -> p (n b)")).then_inc(t_copied, 1)
                fields = OPERANDS_AFTER.get(k, [])
                for f in fields:
                    operands(f)
                    if f != fields[-1]:
                        double(f + 1)
                for g in SPLIT_AFTER.get(k, ()):
                    split(g)
                if fields and fields[-1] + 1 < FIELDS:
                    double(fields[-1] + 1)
                for c in range(summed_after(k - 1) // CHUNK, summed_after(k) // CHUNK):
                    evacuate(c)
                if k == DENSE_AT:
                    act.wait_ge(weights_arrived, 16 * 6)
                    wait_for_k(act, K_GROUPS - 2)
                    nc.scalar.copy(dense_split, dense_sb[:]).then_inc(dense_hi_done, 1)
                    nc.scalar.copy(w1_split, w1_sb[:, CHUNKS, :]).then_inc(dense_hi_done, 1)
            for c in range(summed_after(NUNITS - 1) // CHUNK, CHUNKS):
                evacuate(c)

            for m in range(0, HID1 // P, 2):
                act.wait_ge(h1_ready, m + 1)
                nc.scalar.activation(h1_sb[:, m, :], h1_ps[m], ACT.Relu, bias=b1_sb[:, m:m + 1]).then_inc(
                    h1_act[m], 1)
            act.wait_ge(h2_ready, 1)
            nc.scalar.activation(h2_sb[:, 0, :], h2_ps[0], ACT.Relu, bias=b2_sb[:, 0:1]).then_inc(h2_act[0], 1)
            act.wait_ge(y_ready, 1)
            nc.scalar.copy(y_sb, z_ps[0:1, :]).then_inc(y_done, 1)

        @block.vector
        def _(dve):
            def operands(f):
                if f >= 1:
                    dve.wait_ge(e_hi_done, f)
                    nc.vector.tensor_tensor(
                        e_lo[:, f % M_RING, :], tr_ps[:].rearrange("p t b -> p (t b)"),
                        e_hi[:, f % M_RING, :].bitcast(F32), ALU.subtract).then_inc(e_lo_done, 1)

            def split(g):
                stage = g % K_STAGES
                dve.wait_ge(k_hi_done, g + 1)
                nc.vector.tensor_tensor(k_stage[:, stage], k_stage[:, stage],
                                        k_hi[:, g % SPLIT_RING].bitcast(F32), ALU.subtract).then_inc(k_lo_done, 1)

            for g in range(SPLIT_FIRST):
                split(g)
            for k in range(-1, NUNITS):
                if k >= 0 and not on_pool(k):
                    j, pair, n = UNITS[k]
                    if pair + n == (j + 1) // 2 or pair == 0:
                        dve.wait_ge(e_pair_done, min(2 * (pair + n), j + 1))
                    wait_for_sum(dve, k)
                    dve.wait_ge(t_done, k + 1)
                    bank = UNIT * (k % T_RING)
                    nc.vector.tensor_tensor(
                        prod[:, k % P_RING, 0:n * BATCH], t_ps[:, bank:bank + n, :].rearrange("p n b -> p (n b)"),
                        e_pair[:, pair:pair + n, :].rearrange("p n b -> p (n b)"), ALU.mult).then_inc(prod_done, 1)
                for f in LO_AFTER.get(k, ()):
                    operands(f)
                for g in SPLIT_AFTER.get(k, ()):
                    split(g)
                if k == DENSE_AT:
                    dve.wait_ge(weights_arrived, 16 * 6)
                    dve.wait_ge(dense_hi_done, 2)
                    for quarter in (slice(32, 64), slice(96, 128)):
                        nc.vector.tensor_tensor(dense_split[quarter], dense_sb[quarter],
                                                dense_split[quarter].bitcast(F32), ALU.subtract).then_inc(
                                                    dense_lo_done, 1)
                    nc.vector.tensor_tensor(w1_split[lower], w1_sb[lower, CHUNKS, :],
                                            w1_split[lower].bitcast(F32), ALU.subtract).then_inc(dense_lo_done, 1)

            for m in range(1, HID1 // P, 2):
                dve.wait_ge(h1_ready, m + 1)
                nc.vector.tensor_scalar(h1_sb[:, m, :], h1_ps[m], b1_sb[:, m:m + 1], 0.0, ALU.add,
                                        ALU.max).then_inc(h1_act[m], 1)
            dve.wait_ge(h2_ready, 2)
            nc.vector.tensor_scalar(h2_sb[:, 1, :], h2_ps[1], b2_sb[:, 1:2], 0.0, ALU.add,
                                    ALU.max).then_inc(h2_act[1], 1)

        @block.tensor
        def _(pe):
            def transpose(f):
                if f >= 1:
                    pe.wait_ge(e_pair_done, f)
                if f >= 2:
                    pe.wait_ge(e_lo_done, f - 1)
                pe.wait_ge(doubled, f + 1)
                for t in range(NB):
                    last = nc.tensor.transpose(tr_ps[:, t, :], rows_twice[:, f % 2, t].rearrange("p h e -> p (h e)"),
                                               identity)
                last.then_inc(transposed, 1)

            def sum_up(first):
                chunk, within = divmod(first, CHUNK)
                if chunk and not within:
                    pe.wait_ge(z_done, chunk)
                last_unit = unit_of_block(first + STRIPS - 1)
                pe.wait_ge(prod_done, dve_units(last_unit))
                if pool_units(last_unit):
                    pe.wait_ge(pool_prod_done, pool_units(last_unit))
                r = within // STRIPS
                for s in range(STRIPS):
                    k = unit_of_block(first + s)
                    col = (first + s - FIRST_BLOCK[k]) * BATCH
                    last = nc.tensor.matmul(
                        z_ps[32 * s:32 * s + 32, :], selector[:, SEL_W - 32 - 2 * r:SEL_W - 2 * r],
                        prod[:, k % P_RING, col:col + BATCH], start=(within == 0),
                        stop=(within == CHUNK - STRIPS))
                last.then_inc(summed, 1)

            pe.wait_ge(const_arrived, 16)
            for k in range(-1, NUNITS):
                if k >= 0:
                    j, pair, n = UNITS[k]
                    if pair == 0:
                        pe.wait_ge(e_lo_done, j)
                    if k >= T_RING:
                        if on_pool(k - T_RING):
                            pe.wait_ge(t_copied, pool_units(k - T_RING))
                        else:
                            pe.wait_ge(prod_done, dve_units(k - T_RING))
                    for i in range(n):
                        t = FIRST_BLOCK[k] + i
                        if t % K_GROUP == 0:
                            wait_for_k(pe, t // K_GROUP)
                        tile = k_split[:, t % 2, t // 2 % (K_RING * K_GROUP // 2), :]
                        bank = t_ps[:, UNIT * (k % T_RING) + i, :]
                        nc.tensor.matmul(bank, tile, e_hi[:, j % M_RING, :], start=True, stop=False)
                        last = nc.tensor.matmul(bank, tile, e_lo[:, j % M_RING, :], start=False, stop=True)
                    last.then_inc(t_done, 1)
                for f in OPERANDS_AFTER.get(k, ()):
                    transpose(f)
                for first in range(summed_after(k - 1), summed_after(k), STRIPS):
                    sum_up(first)

            def layer1(m, c):
                cols = slice(m * P, (m + 1) * P)
                if c < 0:
                    return nc.tensor.matmul(h1_ps[m], w1_split[:, cols], dense_split, start=True, stop=False)
                return nc.tensor.matmul(h1_ps[m], w1_sb[:, c, cols], z_sb[:, c, :], start=False,
                                        stop=(c == CHUNKS - 1))

            pe.wait_ge(dense_lo_done, 3)
            pe.wait_ge(e_lo_done, FIELDS - 1)
            for m in range(HID1 // P):
                if m == 1:
                    for first in range(summed_after(NUNITS - 1), NBLOCKS, STRIPS):
                        sum_up(first)
                for c in range(-1, CHUNKS - 1):
                    if m == 0 and c >= 0:
                        pe.wait_ge(z_done, c + 1)
                    layer1(m, c)
            pe.wait_ge(z_done, CHUNKS)
            for m in range(HID1 // P):
                layer1(m, CHUNKS - 1).then_inc(h1_ready, 1)

            for m, c in LAYER2_ORDER:
                if m == 0 or c == 0:
                    pe.wait_ge(h1_act[c], 1)
                last = nc.tensor.matmul(h2_ps[m], w2_sb[:, c, m * P:(m + 1) * P], h1_sb[:, c, :],
                                        start=(c == 0), stop=(c == HID1 // P - 1))
                if c == HID1 // P - 1:
                    last.then_inc(h2_ready, 1)
            for c in range(HID2 // P):
                pe.wait_ge(h2_act[c], 1)
                last = nc.tensor.matmul(z_ps[0:1, :], w3_sb[:, c:c + 1], h2_sb[:, c, :], start=(c == 0),
                                        stop=(c == HID2 // P - 1))
            last.then_inc(y_ready, 1)


def kernel(**inputs):
    import concourse.bacc as bacc
    from concourse.bass_utils import run_bass_kernel_spmd

    pair_index = {}
    for i in range(FIELDS):
        for j in range(i + 1, FIELDS):
            pair_index[i, j] = len(pair_index)

    ids = np.asarray(inputs["ids"]).reshape(NB, P, FIELDS).transpose(1, 2, 0).reshape(P, FIELDS * NB)
    k_in = np.asarray(inputs["L0_rec_kernel"])
    w1_in = np.asarray(inputs["W_top1"])
    k_t = np.zeros((P, NBLOCKS // 2, 2, EMBED), k_in.dtype)
    w1 = np.zeros((CHUNKS + 1, P, HID1), w1_in.dtype)
    for t, (j, pair) in enumerate(BLOCKS):
        for h in range(2):
            i = 2 * pair + h
            if i < j:
                n = pair_index[i, j]
                k_t[64 * (t % 2):64 * (t % 2) + 64, t // 2, h, :] = k_in[:, n, :]
                within = t % CHUNK
                w1[t // CHUNK, 32 * (within % STRIPS) + 2 * (within // STRIPS) + h] = w1_in[n]
    dense_in = np.asarray(inputs["dense_ctx"])
    dense_t = np.zeros((P, BATCH), dense_in.dtype)
    for quarter in range(0, P, 32):
        dense_t[quarter:quarter + DENSE] = dense_in.T
        w1[CHUNKS, quarter:quarter + DENSE] = w1_in[len(pair_index):]
    consts = np.zeros((P, P + SEL_W), np.float32)
    consts[:, 0:P] = np.eye(P)
    consts[0:64, P + 30] = 1.0
    consts[64:128, P + 31] = 1.0

    arrays = {
        "ids": ids,
        **{f"table_{f}": np.asarray(inputs[f"tbl_{f}"]) for f in range(FIELDS)},
        "kernel_t": k_t.reshape(P, NBLOCKS // 2, 2 * EMBED),
        "consts": consts,
        "w1": w1.transpose(1, 0, 2),
        "dense_t": dense_t,
        "b1": np.asarray(inputs["b_top1"]).reshape(HID1 // P, P).T,
        "w2": np.asarray(inputs["W_top2"]).reshape(HID1 // P, P, HID2).transpose(1, 0, 2),
        "b2": np.asarray(inputs["b_top2"]).reshape(HID2 // P, P).T,
        "w3": np.asarray(inputs["W_top3"]).reshape(HID2 // P, P).T,
    }
    arrays = {n: np.ascontiguousarray(a) for n, a in arrays.items()}

    nc = bacc.Bacc("TRN2", target_bir_lowering=False, num_devices=1)
    ap = {n: nc.dram_tensor(n, a.shape, mybir.dt.from_np(a.dtype), kind="ExternalInput").ap()
          for n, a in arrays.items()}
    y = nc.dram_tensor("y", (1, BATCH), F32, kind="ExternalOutput").ap()
    tower(nc, ap["ids"], [ap[f"table_{f}"] for f in range(FIELDS)], ap["kernel_t"], ap["consts"], ap["w1"],
          ap["dense_t"], ap["b1"], ap["w2"], ap["b2"], ap["w3"], y)
    result = run_bass_kernel_spmd(nc, [arrays], core_ids=[0])
    return np.asarray(result.results[0]["y"]).reshape(BATCH, 1)
```

```python
from contextlib import ExitStack

import numpy as np

import concourse.bass as bass
from concourse import mybir
from concourse.alu_op_type import AluOpType as ALU

F32, F32R, I32 = mybir.dt.float32, mybir.dt.float32r, mybir.dt.int32
ACT = mybir.ActivationFunctionType

P = 128
BATCH, FIELDS, EMBED = 512, 32, 64
DENSE, HID1, HID2 = 16, 512, 256
NB = BATCH // P
GROUPS = FIELDS // 2
PSUM_BANKS, BANK = 8, 512

QUADS = FIELDS // 4
MIXED_RING = 2
SLOTS = GROUPS + 2 * MIXED_RING
BLOCKS = []
UNITS = []
UNIT = 2
for _quad in range(QUADS):
    _a, _b, _c, _d = range(4 * _quad, 4 * _quad + 4)
    for _j in (_a, _b, _c, _d):
        for _pair in range(0, 2 * _quad, UNIT):
            BLOCKS += [(_j, (2 * _p, 2 * _p + 1), _p) for _p in range(_pair, _pair + UNIT)]
            UNITS.append((_j, _pair, UNIT))
    _mixed = GROUPS + 2 * (_quad % MIXED_RING)
    BLOCKS += [(_d, (_a, _b), 2 * _quad), (_a, (_c, _b), _mixed), (_c, (_b, _d), _mixed + 1)]
    UNITS += [(_d, 2 * _quad, 1), (_d, _mixed, 2)]
NBLOCKS = len(BLOCKS)
NUNITS = len(UNITS)
FIRST_BLOCK = [sum(u[2] for u in UNITS[:k]) for k in range(NUNITS + 1)]
UNITS_THROUGH = [sum(u[0] <= j for u in UNITS) for j in range(FIELDS)]

CHUNK = 64
CHUNKS = -(-NBLOCKS // CHUNK)
STRIPS = 4
SUMS = 8
DOUBLE_SUMS = 144
SEL_W = 62

K_GROUP = 16
K_GROUPS = -(-NBLOCKS // K_GROUP)
K_STAGES = 3
K_RING = 4
ROW_RING = 16
M_RING = 5
SPLIT_AHEAD = 24
SPLIT_FIRST = 2
SPLIT_RING = 2
T_RING = 3
COPY_RING = 2
P_RING = 9
LAG = 4
LEAD = 3
EARLY, MIDDLE, MIDDLE_LEAD = 4, 12, 2
WEIGHTS_AT = 10
LAYER2_ORDER = [(0, 0), (0, 1), (0, 2), (1, 0), (0, 3), (1, 1), (1, 2), (1, 3)]
DENSE_AT = NUNITS - 10


def unit_of_block(t):
    t = min(t, NBLOCKS - 1)
    return next(k for k in range(NUNITS) if FIRST_BLOCK[k + 1] > t)


MOVED = [max([k + 1 for k in range(NUNITS) for t in range(FIRST_BLOCK[k], FIRST_BLOCK[k + 1])
              if BLOCKS[t][0] == f], default=0) for f in range(FIELDS)]
OPERANDS_AFTER = {-1: [0, 1]}
_at = -1
for _f in range(2, FIELDS):
    _last = UNITS_THROUGH[_f - 1] - 1
    _at = _last if _f <= EARLY else max(_last - (LEAD if _f > MIDDLE else MIDDLE_LEAD), _at)
    OPERANDS_AFTER.setdefault(_at, []).append(_f)
SPLIT_AFTER = {}
for _g in range(SPLIT_FIRST, K_GROUPS):
    _at = unit_of_block(max(K_GROUP * _g - SPLIT_AHEAD, K_GROUP * (_g - K_RING + 1) + 8, 0))
    SPLIT_AFTER.setdefault(_at, []).append(_g)


def summed_after(k):
    now, before = (FIRST_BLOCK[max(i - LAG + 1, 0)] for i in (k, k - 1))
    now, before = (n // SUMS * SUMS if n >= DOUBLE_SUMS else n // STRIPS * STRIPS for n in (now, before))
    if now // CHUNK > before // CHUNK:
        now = now // CHUNK * CHUNK
    return min(now, NBLOCKS)


FIRST_ON_POOL = 75
POOL_EVERY = 3


def on_pool(k):
    return k >= FIRST_ON_POOL and k % POOL_EVERY == POOL_EVERY - 1


def pool_units(k):
    return sum(on_pool(i) for i in range(k + 1))


def dve_units(k):
    return k + 1 - pool_units(k)


def tower(nc, ids, tables, kernel_t, consts, w1, dense_t, b1, w2, b2, w3, y):
    ctx = ExitStack()
    with ctx:
        def sb(name, shape, dt=F32):
            return ctx.enter_context(nc.sbuf_tensor(name, shape, dt))

        def ps(name, shape):
            return ctx.enter_context(nc.psum_tensor(name, shape, F32))

        def sem(name):
            return ctx.enter_context(nc.semaphore(name))

        idx = sb("idx", [P, FIELDS * NB], I32)
        rows = sb("rows", [P, ROW_RING, NB, EMBED])
        const = sb("const", [P, P + SEL_W])
        identity, selector = const[:, 0:P], const[:, P:P + SEL_W]
        rows_twice = sb("rows_twice", [P, 2, NB, 2, EMBED])
        e_pair = sb("e_pair", [P, SLOTS, BATCH])
        e_hi = sb("e_hi", [P, M_RING, BATCH], F32R)
        e_lo = sb("e_lo", [P, M_RING, BATCH], F32R)
        k_stage = sb("k_stage", [P, K_STAGES, K_GROUP // 2, P])
        k_hi = sb("k_hi", [P, SPLIT_RING, K_GROUP // 2, P], F32R)
        k_split = sb("k_split", [P, 2, K_RING * K_GROUP // 2, P], F32R)
        t_copy = sb("t_copy", [P, COPY_RING, UNIT * BATCH])
        prod = sb("prod", [P, P_RING, UNIT * BATCH])
        z_sb = sb("z_sb", [P, CHUNKS, BATCH])
        dense_sb = sb("dense_sb", [P, BATCH])
        w1_sb = sb("w1_sb", [P, CHUNKS + 1, HID1])
        w2_sb = sb("w2_sb", [P, HID1 // P, HID2])
        w3_sb = sb("w3_sb", [P, HID2 // P])
        b1_sb = sb("b1_sb", [P, HID1 // P])
        b2_sb = sb("b2_sb", [P, HID2 // P])
        h1_sb = rows[:, 0:8].rearrange("p (m f) t e -> p m (f t e)", m=4)
        h2_sb = rows[:, 8:12].rearrange("p (m f) t e -> p m (f t e)", m=2)
        free_split = k_hi[:, (K_GROUPS - 2) % SPLIT_RING].rearrange("p t c -> p (t c)")
        dense_split, w1_split = free_split[:, 0:BATCH], free_split[:, BATCH:BATCH + HID1]
        y_sb = dense_sb[0:1, :]

        t_ps = ps("t_ps", [P, T_RING * UNIT, BANK])
        tr_ps = ps("tr_ps", [P, NB, P])
        z_ps = ps("z_ps", [P, BANK])
        h1_ps = [tr_ps[:].rearrange("p t b -> p (t b)")] + [t_ps[:, m, :] for m in range(1, HID1 // P)]
        h2_ps = [t_ps[:, 4, :], t_ps[:, 5, :]]

        ids_arrived = sem("ids_arrived")
        const_arrived = sem("const_arrived")
        weights_arrived = sem("weights_arrived")
        rows_arrived = [sem(f"rows_arrived_{f}") for f in range(FIELDS)]
        k_arrived = [sem(f"k_arrived_{s}") for s in range(K_STAGES)]
        k_hi_done = sem("k_hi_done")
        k_lo_done = sem("k_lo_done")
        k_spread = [sem(f"k_spread_{s}") for s in range(K_STAGES)]
        doubled = sem("doubled")
        transposed = sem("transposed")
        e_hi_done = sem("e_hi_done")
        e_pair_done = sem("e_pair_done")
        mixed_done = sem("mixed_done")
        e_lo_done = sem("e_lo_done")
        t_done = sem("t_done")
        t_copied = sem("t_copied")
        prod_done = sem("prod_done")
        pool_prod_done = sem("pool_prod_done")
        summed = sem("summed")
        z_done = sem("z_done")
        dense_hi_done, dense_lo_done = sem("dense_hi_done"), sem("dense_lo_done")
        h1_ready, h1_act = sem("h1_ready"), [sem(f"h1_act_{m}") for m in range(HID1 // P)]
        h2_ready, h2_act = sem("h2_ready"), [sem(f"h2_act_{m}") for m in range(HID2 // P)]
        y_ready, y_done, y_stored = sem("y_ready"), sem("y_done"), sem("y_stored")
        block = ctx.enter_context(nc.Block())

        upper, lower = slice(0, 64), slice(64, 128)

        def ring_of(g):
            first = (g % K_RING) * (K_GROUP // 2)
            return slice(first, first + K_GROUP // 2)

        def wait_for_k(engine, g):
            engine.wait_ge(k_spread[g % K_STAGES], 16 * 4 * (g // K_STAGES + 1))

        def wait_for_sum(engine, k):
            if k >= P_RING:
                engine.wait_ge(summed, -(-FIRST_BLOCK[k - P_RING + 1] // STRIPS))

        def wait_for_products(engine, k):
            engine.wait_ge(prod_done, dve_units(k))
            if pool_units(k):
                engine.wait_ge(pool_prod_done, pool_units(k))

        def freed_units(g):
            return unit_of_block(K_GROUP * (g - K_RING + 1) - 1) + 1

        @block.sync
        def _(sp):
            sp.dma_start(idx[:], ids).then_inc(ids_arrived, 16)
            sp.dma_start(const[:], consts).then_inc(const_arrived, 16)
            def load(g):
                n = K_GROUP // 2
                if g >= K_STAGES:
                    wait_for_k(sp, g - K_STAGES)
                sp.dma_start(k_stage[:, g % K_STAGES], kernel_t[:, g * n:(g + 1) * n, :]).then_inc(
                    k_arrived[g % K_STAGES], 16)

            def spread_kernel(g):
                at, stage, done = ring_of(g), g % K_STAGES, k_spread[g % K_STAGES]
                k_raw, hi = k_split[:].bitcast(F32), k_hi[:].bitcast(F32)
                if g >= K_RING:
                    sp.wait_ge(t_done, freed_units(g))
                sp.wait_ge(k_hi_done, g + 1)
                sp.dma_start(k_raw[upper, 0, at, :], hi[upper, g % SPLIT_RING]).then_inc(done, 16)
                sp.dma_start(k_raw[lower, 1, at, :], hi[lower, g % SPLIT_RING]).then_inc(done, 16)
                sp.wait_ge(k_lo_done, g + 1)
                sp.dma_start(k_raw[lower, 0, at, :], k_stage[upper, stage]).then_inc(done, 16)
                sp.dma_start(k_raw[upper, 1, at, :], k_stage[lower, stage]).then_inc(done, 16)

            for g in range(K_STAGES):
                load(g)
            for g in range(K_GROUPS):
                spread_kernel(g)
                if 0 <= g - 1 < K_GROUPS - K_STAGES:
                    load(g - 1 + K_STAGES)
                if g == WEIGHTS_AT:
                    for dst, src in ((w1_sb, w1), (w2_sb, w2), (w3_sb, w3), (b1_sb, b1), (b2_sb, b2),
                                     (dense_sb, dense_t)):
                        sp.dma_start(dst[:], src).then_inc(weights_arrived, 16)
            sp.wait_ge(y_done, 1)
            sp.dma_start(y, y_sb).then_inc(y_stored, 16)
            sp.wait_ge(y_stored, 16)

        @block.gpsimd
        def _(pool):
            pool.wait_ge(ids_arrived, 16)
            for f in range(FIELDS):
                if f >= ROW_RING:
                    pool.wait_ge(doubled, f - ROW_RING + 1)
                for t in range(NB):
                    at = f * NB + t
                    nc.gpsimd.indirect_dma_start(
                        out=rows[:, f % ROW_RING, t, :], out_offset=None, in_=tables[f],
                        in_offset=bass.IndirectOffsetOnAxis(ap=idx[:, at:at + 1], axis=0),
                    ).then_inc(rows_arrived[f], 16)
            for f in range(FIELDS):
                pool.wait_ge(rows_arrived[f], 16 * NB)
            for k in range(NUNITS):
                if on_pool(k):
                    j, pair, n = UNITS[k]
                    if pair >= GROUPS:
                        pool.wait_ge(mixed_done, 4 * (j // 4 + 1))
                    pool.wait_ge(t_copied, pool_units(k))
                    wait_for_sum(pool, k)
                    nc.gpsimd.tensor_tensor(
                        prod[:, k % P_RING, 0:n * BATCH], t_copy[:, pool_units(k) % COPY_RING, 0:n * BATCH],
                        e_pair[:, pair:pair + n, :].rearrange("p n b -> p (n b)"), ALU.mult).then_inc(
                            pool_prod_done, 1)

        @block.scalar
        def _(act):
            def double(f):
                act.wait_ge(rows_arrived[f], 16 * NB)
                if f >= 2:
                    act.wait_ge(transposed, f - 1)
                nc.scalar.copy(rows_twice[:, f % 2],
                               rows[:, f % ROW_RING].unsqueeze(2).broadcast_to([P, NB, 2, EMBED])).then_inc(doubled, 1)

            def operands(f):
                act.wait_ge(transposed, f + 1)
                half = slice(64 * (f % 2), 64 * (f % 2) + 64)
                nc.scalar.copy(e_pair[half, f // 2, :], tr_ps[half].rearrange("p t b -> p (t b)")).then_inc(
                    e_pair_done, 1)
                quad, place = divmod(f, 4)
                mixed = GROUPS + 2 * (quad % MIXED_RING)
                if place == 1:
                    if quad >= MIXED_RING:
                        wait_for_products(act, UNITS_THROUGH[4 * (quad - MIXED_RING) + 3] - 1)
                    nc.scalar.copy(e_pair[upper, mixed + 1, :], tr_ps[upper].rearrange("p t b -> p (t b)")).then_inc(
                        mixed_done, 1)
                if f >= M_RING and MOVED[f - M_RING]:
                    act.wait_ge(t_done, MOVED[f - M_RING])
                nc.scalar.copy(e_hi[:, f % M_RING, :], tr_ps[:].rearrange("p t b -> p (t b)")).then_inc(
                    e_hi_done, 1)
                if place:
                    slot = mixed + (place == 3)
                    act.wait_ge(e_pair_done, f + 1)
                    nc.scalar.copy(e_pair[half, slot, :], e_pair[half, f // 2, :]).then_inc(mixed_done, 1)

            def split(g):
                stage = g % K_STAGES
                act.wait_ge(k_arrived[stage], 16 * (g // K_STAGES + 1))
                if g >= SPLIT_RING:
                    wait_for_k(act, g - SPLIT_RING)
                nc.scalar.copy(k_hi[:, g % SPLIT_RING], k_stage[:, stage]).then_inc(k_hi_done, 1)

            for g in range(SPLIT_FIRST):
                split(g)
            def evacuate(c):
                act.wait_ge(summed, min((c + 1) * CHUNK, NBLOCKS) // STRIPS)
                nc.scalar.copy(z_sb[:, c, :], z_ps[:]).then_inc(z_done, 1)

            double(0)
            for k in range(-1, NUNITS):
                if k >= 0 and on_pool(k):
                    n = UNITS[k][2]
                    bank = UNIT * (k % T_RING)
                    act.wait_ge(t_done, k + 1)
                    if pool_units(k) > COPY_RING:
                        act.wait_ge(pool_prod_done, pool_units(k) - COPY_RING)
                    nc.scalar.copy(t_copy[:, pool_units(k) % COPY_RING, 0:n * BATCH],
                                   t_ps[:, bank:bank + n, :].rearrange("p n b -> p (n b)")).then_inc(t_copied, 1)
                fields = OPERANDS_AFTER.get(k, [])
                for f in fields:
                    operands(f)
                    if f != fields[-1]:
                        double(f + 1)
                for g in SPLIT_AFTER.get(k, ()):
                    split(g)
                if fields and fields[-1] + 1 < FIELDS:
                    double(fields[-1] + 1)
                for c in range(summed_after(k - 1) // CHUNK, summed_after(k) // CHUNK):
                    evacuate(c)
                if k == DENSE_AT:
                    act.wait_ge(weights_arrived, 16 * 6)
                    wait_for_k(act, K_GROUPS - 2)
                    nc.scalar.copy(dense_split, dense_sb[:]).then_inc(dense_hi_done, 1)
                    nc.scalar.copy(w1_split, w1_sb[:, CHUNKS, :]).then_inc(dense_hi_done, 1)
            for c in range(summed_after(NUNITS - 1) // CHUNK, CHUNKS):
                evacuate(c)

            for m in range(0, HID1 // P, 2):
                act.wait_ge(h1_ready, m + 1)
                nc.scalar.activation(h1_sb[:, m, :], h1_ps[m], ACT.Relu, bias=b1_sb[:, m:m + 1]).then_inc(
                    h1_act[m], 1)
            act.wait_ge(h2_ready, 1)
            nc.scalar.activation(h2_sb[:, 0, :], h2_ps[0], ACT.Relu, bias=b2_sb[:, 0:1]).then_inc(h2_act[0], 1)
            act.wait_ge(y_ready, 1)
            nc.scalar.copy(y_sb, z_ps[0:1, :]).then_inc(y_done, 1)

        @block.vector
        def _(dve):
            def operands(f):
                dve.wait_ge(e_hi_done, f + 1)
                nc.vector.tensor_tensor(
                    e_lo[:, f % M_RING, :], tr_ps[:].rearrange("p t b -> p (t b)"),
                    e_hi[:, f % M_RING, :].bitcast(F32), ALU.subtract).then_inc(e_lo_done, 1)

            def split(g):
                stage = g % K_STAGES
                dve.wait_ge(k_hi_done, g + 1)
                nc.vector.tensor_tensor(k_stage[:, stage], k_stage[:, stage],
                                        k_hi[:, g % SPLIT_RING].bitcast(F32), ALU.subtract).then_inc(k_lo_done, 1)

            for g in range(SPLIT_FIRST):
                split(g)
            for k in range(-1, NUNITS):
                if k >= 0 and not on_pool(k):
                    j, pair, n = UNITS[k]
                    if pair >= GROUPS:
                        dve.wait_ge(mixed_done, 4 * (j // 4 + 1))
                    elif k == 0 or UNITS[k - 1][0] != j:
                        dve.wait_ge(e_pair_done, j // 2 * 2)
                    wait_for_sum(dve, k)
                    dve.wait_ge(t_done, k + 1)
                    bank = UNIT * (k % T_RING)
                    nc.vector.tensor_tensor(
                        prod[:, k % P_RING, 0:n * BATCH], t_ps[:, bank:bank + n, :].rearrange("p n b -> p (n b)"),
                        e_pair[:, pair:pair + n, :].rearrange("p n b -> p (n b)"), ALU.mult).then_inc(prod_done, 1)
                for f in OPERANDS_AFTER.get(k, ()):
                    operands(f)
                for g in SPLIT_AFTER.get(k, ()):
                    split(g)
                if k == DENSE_AT:
                    dve.wait_ge(weights_arrived, 16 * 6)
                    dve.wait_ge(dense_hi_done, 2)
                    for quarter in (slice(32, 64), slice(96, 128)):
                        nc.vector.tensor_tensor(dense_split[quarter], dense_sb[quarter],
                                                dense_split[quarter].bitcast(F32), ALU.subtract).then_inc(
                                                    dense_lo_done, 1)
                    nc.vector.tensor_tensor(w1_split[lower], w1_sb[lower, CHUNKS, :],
                                            w1_split[lower].bitcast(F32), ALU.subtract).then_inc(dense_lo_done, 1)

            for m in range(1, HID1 // P, 2):
                dve.wait_ge(h1_ready, m + 1)
                nc.vector.tensor_scalar(h1_sb[:, m, :], h1_ps[m], b1_sb[:, m:m + 1], 0.0, ALU.add,
                                        ALU.max).then_inc(h1_act[m], 1)
            dve.wait_ge(h2_ready, 2)
            nc.vector.tensor_scalar(h2_sb[:, 1, :], h2_ps[1], b2_sb[:, 1:2], 0.0, ALU.add,
                                    ALU.max).then_inc(h2_act[1], 1)

        @block.tensor
        def _(pe):
            def transpose(f):
                if f >= 1:
                    pe.wait_ge(e_lo_done, f)
                pe.wait_ge(doubled, f + 1)
                for t in range(NB):
                    last = nc.tensor.transpose(tr_ps[:, t, :], rows_twice[:, f % 2, t].rearrange("p h e -> p (h e)"),
                                               identity)
                last.then_inc(transposed, 1)

            def sum_up(first):
                chunk, within = divmod(first, CHUNK)
                if chunk and not within:
                    pe.wait_ge(z_done, chunk)
                wait_for_products(pe, unit_of_block(first + STRIPS - 1))
                r = within // STRIPS
                for s in range(STRIPS):
                    k = unit_of_block(first + s)
                    col = (first + s - FIRST_BLOCK[k]) * BATCH
                    last = nc.tensor.matmul(
                        z_ps[32 * s:32 * s + 32, :], selector[:, SEL_W - 32 - 2 * r:SEL_W - 2 * r],
                        prod[:, k % P_RING, col:col + BATCH], start=(within == 0),
                        stop=(within == CHUNK - STRIPS or first == NBLOCKS - STRIPS))
                last.then_inc(summed, 1)

            pe.wait_ge(const_arrived, 16)
            for k in range(-1, NUNITS):
                if k >= 0:
                    j, pair, n = UNITS[k]
                    if k == 0 or UNITS[k - 1][0] != j:
                        pe.wait_ge(e_lo_done, j + 1)
                    if k >= T_RING:
                        if on_pool(k - T_RING):
                            pe.wait_ge(t_copied, pool_units(k - T_RING))
                        else:
                            pe.wait_ge(prod_done, dve_units(k - T_RING))
                    for i in range(n):
                        t = FIRST_BLOCK[k] + i
                        if t % K_GROUP == 0:
                            wait_for_k(pe, t // K_GROUP)
                        tile = k_split[:, t % 2, t // 2 % (K_RING * K_GROUP // 2), :]
                        bank = t_ps[:, UNIT * (k % T_RING) + i, :]
                        moving = BLOCKS[t][0] % M_RING
                        nc.tensor.matmul(bank, tile, e_hi[:, moving, :], start=True, stop=False)
                        last = nc.tensor.matmul(bank, tile, e_lo[:, moving, :], start=False, stop=True)
                    last.then_inc(t_done, 1)
                for f in OPERANDS_AFTER.get(k, ()):
                    transpose(f)
                for first in range(summed_after(k - 1), summed_after(k), STRIPS):
                    sum_up(first)

            def layer1(m, c):
                cols = slice(m * P, (m + 1) * P)
                if c < 0:
                    return nc.tensor.matmul(h1_ps[m], w1_split[:, cols], dense_split, start=True, stop=False)
                return nc.tensor.matmul(h1_ps[m], w1_sb[:, c, cols], z_sb[:, c, :], start=False,
                                        stop=(c == CHUNKS - 1))

            pe.wait_ge(dense_lo_done, 3)
            pe.wait_ge(e_lo_done, FIELDS)
            for m in range(HID1 // P):
                if m == 1:
                    for first in range(summed_after(NUNITS - 1), NBLOCKS, STRIPS):
                        sum_up(first)
                for c in range(-1, CHUNKS - 1):
                    if m == 0 and c >= 0:
                        pe.wait_ge(z_done, c + 1)
                    layer1(m, c)
            pe.wait_ge(z_done, CHUNKS)
            for m in range(HID1 // P):
                layer1(m, CHUNKS - 1).then_inc(h1_ready, 1)

            for m, c in LAYER2_ORDER:
                if m == 0 or c == 0:
                    pe.wait_ge(h1_act[c], 1)
                last = nc.tensor.matmul(h2_ps[m], w2_sb[:, c, m * P:(m + 1) * P], h1_sb[:, c, :],
                                        start=(c == 0), stop=(c == HID1 // P - 1))
                if c == HID1 // P - 1:
                    last.then_inc(h2_ready, 1)
            for c in range(HID2 // P):
                pe.wait_ge(h2_act[c], 1)
                last = nc.tensor.matmul(z_ps[0:1, :], w3_sb[:, c:c + 1], h2_sb[:, c, :], start=(c == 0),
                                        stop=(c == HID2 // P - 1))
            last.then_inc(y_ready, 1)


def kernel(**inputs):
    import concourse.bacc as bacc
    from concourse.bass_utils import run_bass_kernel_spmd

    pair_index = {}
    for i in range(FIELDS):
        for j in range(i + 1, FIELDS):
            pair_index[i, j] = len(pair_index)

    ids = np.asarray(inputs["ids"]).reshape(NB, P, FIELDS).transpose(1, 2, 0).reshape(P, FIELDS * NB)
    k_in = np.asarray(inputs["L0_rec_kernel"])
    w1_in = np.asarray(inputs["W_top1"])
    k_t = np.zeros((P, K_GROUPS * K_GROUP // 2, 2, EMBED), k_in.dtype)
    w1 = np.zeros((CHUNKS + 1, P, HID1), w1_in.dtype)
    for t, (j, met, _) in enumerate(BLOCKS):
        within = t % CHUNK
        for h, i in enumerate(met):
            n = pair_index[min(i, j), max(i, j)]
            tile = k_in[:, n, :] if i < j else k_in[:, n, :].T
            k_t[64 * (t % 2):64 * (t % 2) + 64, t // 2, h, :] = tile
            w1[t // CHUNK, 32 * (within % STRIPS) + 2 * (within // STRIPS) + h] = w1_in[n]
    dense_in = np.asarray(inputs["dense_ctx"])
    dense_t = np.zeros((P, BATCH), dense_in.dtype)
    for quarter in range(0, P, 32):
        dense_t[quarter:quarter + DENSE] = dense_in.T
        w1[CHUNKS, quarter:quarter + DENSE] = w1_in[len(pair_index):]
    consts = np.zeros((P, P + SEL_W), np.float32)
    consts[:, 0:P] = np.eye(P)
    consts[0:64, P + 30] = 1.0
    consts[64:128, P + 31] = 1.0

    arrays = {
        "ids": ids,
        **{f"table_{f}": np.asarray(inputs[f"tbl_{f}"]) for f in range(FIELDS)},
        "kernel_t": k_t.reshape(P, K_GROUPS * K_GROUP // 2, 2 * EMBED),
        "consts": consts,
        "w1": w1.transpose(1, 0, 2),
        "dense_t": dense_t,
        "b1": np.asarray(inputs["b_top1"]).reshape(HID1 // P, P).T,
        "w2": np.asarray(inputs["W_top2"]).reshape(HID1 // P, P, HID2).transpose(1, 0, 2),
        "b2": np.asarray(inputs["b_top2"]).reshape(HID2 // P, P).T,
        "w3": np.asarray(inputs["W_top3"]).reshape(HID2 // P, P).T,
    }
    arrays = {n: np.ascontiguousarray(a) for n, a in arrays.items()}

    nc = bacc.Bacc("TRN2", target_bir_lowering=False, num_devices=1)
    ap = {n: nc.dram_tensor(n, a.shape, mybir.dt.from_np(a.dtype), kind="ExternalInput").ap()
          for n, a in arrays.items()}
    y = nc.dram_tensor("y", (1, BATCH), F32, kind="ExternalOutput").ap()
    tower(nc, ap["ids"], [ap[f"table_{f}"] for f in range(FIELDS)], ap["kernel_t"], ap["consts"], ap["w1"],
          ap["dense_t"], ap["b1"], ap["w2"], ap["b2"], ap["w3"], y)
    result = run_bass_kernel_spmd(nc, [arrays], core_ids=[0])
    return np.asarray(result.results[0]["y"]).reshape(BATCH, 1)
```
